# Optimizing a Trainium2 kernel written in Bass

```python
import numpy as np
import jax
import jax.numpy as jnp

def _softmax(x, axis=-1):
    return jax.nn.softmax(x, axis=axis)

def _gelu(x):
    return jax.nn.gelu(x, approximate=True)

def _silu(x):
    return jax.nn.silu(x)

def _sigmoid(x):
    return jax.nn.sigmoid(x)

def _layernorm(x, axis=-1, eps=1e-05):
    m = jnp.mean(x, axis=axis, keepdims=True)
    v = jnp.var(x, axis=axis, keepdims=True)
    return (x - m) / jnp.sqrt(v + eps)

def _scatter_add(tgt, idx, src, axis=0):
    return tgt.at[idx].add(src)

def _segment_sum(src, seg, n):
    return jax.ops.segment_sum(src, seg, n)
kernel_name = 'mk_adaln_ffn_d1_seqx_r8_23d704'

def setup_inputs(seed: int=0):
    np.random.seed(seed)
    _w = jnp.asarray

    def _rec_inputs():
        import jax
        import jax.numpy as jnp
        _rk = jax.random.key(seed)
        x = -7.109e-05 + 0.9999 * jax.random.normal(jax.random.fold_in(_rk, 1), (64, 32, 256), jnp.float32)
        _lenS = 32 - jax.random.randint(jax.random.fold_in(_rk, 7), (64,), 0, max(1, 32 // 4) + 1, jnp.int32)
        _lenS2 = 32 - jax.random.randint(jax.random.fold_in(_rk, 8), (64,), 0, max(1, 32 // 4) + 1, jnp.int32)
        itok_B_1_198 = jax.random.randint(jax.random.fold_in(_rk, 11), (64,), 1, 199, jnp.int32)
        return (x, itok_B_1_198)
    x, itok_B_1_198 = _rec_inputs()

    def _L0_cond_setup():
        import jax, jax.numpy as jnp
        import numpy as np
        B, C, T = (128, 32, 256)
        S, D = (200, 32)
        key = jax.random.key(seed)
        k1, k2, k3 = jax.random.split(key, 3)
        x = jax.random.normal(k1, (B, C, T), dtype=jnp.float32)
        conditions = jax.random.randint(k2, (B,), 0, S, dtype=jnp.int64)
        weights = jax.random.normal(k3, (S, C, D), dtype=jnp.float32) / jnp.sqrt(jnp.float32(C))
        return {'x': x, 'conditions': conditions, 'weights': weights}
    _L0_cond_all = _L0_cond_setup()
    _L0_cond_in = {k: v for k, v in _L0_cond_all.items() if k in ('weights',)}
    del _L0_cond_all

    def _L0_ffn_setup():
        import jax, jax.numpy as jnp
        import numpy as np
        B, S, H = (4, 256, 256)
        INTER = 512
        E = 8
        TOPK = 2
        SHARED_I = INTER * 2

        def moe_forward(hidden_states, router_w, w1, w2, w_gate, w_up, w_down):
            b, s, h = hidden_states.shape
            x = hidden_states.reshape(-1, h)
            T = x.shape[0]
            logits = x @ router_w
            top_logits, top_indices = jax.lax.top_k(logits, TOPK)
            scores = jax.nn.softmax(top_logits, axis=-1)
            flat_idx = top_indices.reshape(-1)
            sorted_pos = jnp.argsort(flat_idx, stable=True)
            permuted = x[sorted_pos // TOPK]
            expert_ids = flat_idx[sorted_pos]
            out = jnp.zeros((T * TOPK, h), x.dtype)
            for e in range(E):
                mask = (expert_ids == e)[:, None]
                f1 = permuted * mask @ w1[e]
                g, u = jnp.split(f1, 2, axis=-1)
                act = jax.nn.silu(g) * u
                out = out + jnp.where(mask, act @ w2[e], 0.0)
            unperm = jnp.zeros_like(out).at[sorted_pos].set(out)
            combined = (unperm.reshape(T, TOPK, h) * scores[..., None]).sum(axis=1)
            shared = jax.nn.silu(x @ w_gate) * (x @ w_up) @ w_down
            return (combined + shared).reshape(b, s, h)
        key = jax.random.key(seed)
        ks = jax.random.split(key, 7)
        s = 0.02
        return {'hidden_states': jax.random.normal(ks[0], (B, S, H), jnp.float32), 'router_w': jax.random.normal(ks[1], (H, E), jnp.float32) * s, 'w1': jax.random.normal(ks[2], (E, H, 2 * INTER), jnp.float32) * s, 'w2': jax.random.normal(ks[3], (E, INTER, H), jnp.float32) * s, 'w_gate': jax.random.normal(ks[4], (H, SHARED_I), jnp.float32) * s, 'w_up': jax.random.normal(ks[5], (H, SHARED_I), jnp.float32) * s, 'w_down': jax.random.normal(ks[6], (SHARED_I, H), jnp.float32) * s}
    _L0_ffn_all = _L0_ffn_setup()
    _L0_ffn_in = {k: v for k, v in _L0_ffn_all.items() if k in ('router_w', 'w1', 'w2', 'w_gate', 'w_up', 'w_down')}
    del _L0_ffn_all
    return {'x': x, 'itok_B_1_198': itok_B_1_198, 'L0_cond_weights': _L0_cond_in['weights'], 'L0_ffn_router_w': _L0_ffn_in['router_w'], 'L0_ffn_w1': _L0_ffn_in['w1'], 'L0_ffn_w2': _L0_ffn_in['w2'], 'L0_ffn_w_gate': _L0_ffn_in['w_gate'], 'L0_ffn_w_up': _L0_ffn_in['w_up'], 'L0_ffn_w_down': _L0_ffn_in['w_down']}

def reference(x, itok_B_1_198, L0_cond_weights, L0_ffn_router_w, L0_ffn_w1, L0_ffn_w2, L0_ffn_w_gate, L0_ffn_w_up, L0_ffn_w_down):
    import jax
    import jax.numpy as jnp

    def _L0_cond_ref(x, conditions, weights):
        import jax, jax.numpy as jnp
        import numpy as np
        B, C, T = (128, 32, 256)
        S, D = (200, 32)
        w = weights[conditions]
        return jnp.einsum('bct,bcd->bdt', x, w)

    def _L0_ffn_ref(hidden_states, router_w, w1, w2, w_gate, w_up, w_down):
        import jax, jax.numpy as jnp
        import numpy as np
        B, S, H = (4, 256, 256)
        INTER = 512
        E = 8
        TOPK = 2
        SHARED_I = INTER * 2

        def moe_forward(hidden_states, router_w, w1, w2, w_gate, w_up, w_down):
            b, s, h = hidden_states.shape
            x = hidden_states.reshape(-1, h)
            T = x.shape[0]
            logits = x @ router_w
            top_logits, top_indices = jax.lax.top_k(logits, TOPK)
            scores = jax.nn.softmax(top_logits, axis=-1)
            flat_idx = top_indices.reshape(-1)
            sorted_pos = jnp.argsort(flat_idx, stable=True)
            permuted = x[sorted_pos // TOPK]
            expert_ids = flat_idx[sorted_pos]
            out = jnp.zeros((T * TOPK, h), x.dtype)
            for e in range(E):
                mask = (expert_ids == e)[:, None]
                f1 = permuted * mask @ w1[e]
                g, u = jnp.split(f1, 2, axis=-1)
                act = jax.nn.silu(g) * u
                out = out + jnp.where(mask, act @ w2[e], 0.0)
            unperm = jnp.zeros_like(out).at[sorted_pos].set(out)
            combined = (unperm.reshape(T, TOPK, h) * scores[..., None]).sum(axis=1)
            shared = jax.nn.silu(x @ w_gate) * (x @ w_up) @ w_down
            return (combined + shared).reshape(b, s, h)
        return moe_forward(hidden_states, router_w, w1, w2, w_gate, w_up, w_down)
    x = x + _L0_ffn_ref(_L0_cond_ref(x, itok_B_1_198, L0_cond_weights), L0_ffn_router_w, L0_ffn_w1, L0_ffn_w2, L0_ffn_w_gate, L0_ffn_w_up, L0_ffn_w_down)
    return x

_drawn_inputs = setup_inputs


def setup_inputs(seed=0):
    import zlib

    import numpy as np

    out = dict(_drawn_inputs(seed))
    spreads = {}
    factors = {'L0_ffn_router_w': 3.728, 'L0_ffn_w1': 3.224, 'L0_ffn_w2': 3.227}
    for name, (base, spread) in spreads.items():
        noise = np.random.default_rng([zlib.crc32(name.encode()), seed]).standard_normal(out[name].shape)
        drawn = base * np.exp(spread * noise) if base else spread * noise
        out[name] = jnp.asarray(drawn.astype(out[name].dtype))
    for name, factor in factors.items():
        out[name] = (out[name] * factor).astype(out[name].dtype)
    return out
```

```python
from contextlib import ExitStack

import concourse.bass as bass
from concourse import mybir

ALU = mybir.AluOpType
ACT = mybir.ActivationFunctionType
AX = mybir.AxisListType
F32 = mybir.dt.float32
F32R = mybir.dt.float32r
BF16 = mybir.dt.bfloat16
I32 = mybir.dt.int32


def cond_moe_ffn(nc, x, itok, cond_w, router_w, w1, w2, w_gate, w_up, w_down, out):
    P = 128
    B, C, H = x.shape
    T = B * C
    NG = T // P
    BPG = P // C
    KC = H // P
    E = router_w.shape[1]
    INTER = w2.shape[1]
    IC = INTER // P
    SH = w_gate.shape[1]
    SC = SH // P
    BLK = 512
    GB = BLK // P
    NBLK = T // BLK
    HALF = NBLK // 2
    TOPK = 2
    NT = TOPK * T // P + E - 1
    TRIO = 3
    MAXT = T // P
    S1 = HALF * SC
    S2 = S1 + NT
    WCOL = KC * 2 * INTER
    ECOL = WCOL + IC * H
    NGB = 16
    GWAY = NGB // TOPK
    assert NT % TRIO == 0 and P % C == 0 and 2 * INTER == 1024 and BLK == INTER and SH % P == 0

    x_rows = x.rearrange("b c t -> (b c) t").rearrange("(g p) t -> p g t", p=P)
    out_rows = out.rearrange("b c t -> (b c) t").rearrange("(g p) t -> p g t", p=P)
    y_slots = nc.dram_tensor("y_slots", [(NT + 1) * P, H], F32).ap()
    cond_rows = nc.dram_tensor("cond_rows", [B, C * C], F32).ap()
    o_slots = nc.dram_tensor("o_slots", [NT * P, H], F32).ap()

    with ExitStack() as ctx:
        def sb(name, shape, dt=F32):
            return ctx.enter_context(nc.sbuf_tensor(name, shape, dt))

        def psum(name):
            return ctx.enter_context(nc.psum_tensor(name, [P, 512], F32))

        def sem(name):
            return ctx.enter_context(nc.semaphore(name))

        x_sb = sb("x_sb", [P, NG, H])
        y_sb = sb("y_sb", [P, NG, H])
        yt_h = sb("yt_h", [P, KC, T], F32R)
        yt_l = sb("yt_l", [P, KC, T], F32R)
        gu_h = sb("gu_h", [P, KC, 2 * SH], F32R)
        gu_l = sb("gu_l", [P, KC, 2 * SH], F32R)
        wd_h = sb("wd_h", [P, SC, H], F32R)
        wd_l = sb("wd_l", [P, SC, H], F32R)
        ew_h = sb("ew_h", [P, 2, ECOL], F32R)
        ew_l = sb("ew_l", [P, 2, ECOL], F32R)
        stage = sb("stage", [P, ECOL])
        raw_a = sb("raw_a", [P, KC, SH])
        arena = sb("arena", [P, 2 * 512 + 6 * H])
        xt_h = sb("xt_h", [P, KC, P], F32R)
        xt_l = sb("xt_l", [P, KC, P], F32R)
        at_h = sb("at_h", [P, 2, 512], F32R)
        at_l = sb("at_l", [P, 2, 512], F32R)
        zero = sb("zero", [P, H])
        ident = sb("ident", [P, P])
        rt_raw = sb("rt_raw", [P, KC, E])
        rt_h = sb("rt_h", [P, KC, P], F32R)
        rt_l = sb("rt_l", [P, KC, P], F32R)
        itok_sb = sb("itok_sb", [B, 1], I32)

        cond_blk = stage[:, 0:NG * P].rearrange("p (g q) -> p g q", g=NG)
        lgt = [arena[0:E, 1024 + b * BLK:1024 + (b + 1) * BLK] if b < 2 else
               stage[0:E, NG * P + (b - 2) * BLK:NG * P + (b - 1) * BLK] for b in range(NBLK)]
        cond_sb = y_sb[0:B, 0:C * C // H, :].rearrange("b g h -> b (g h)")
        raw_b = arena[:, 0:KC * SH].rearrange("p (k n) -> p k n", k=KC)
        silu_sb = arena[:, 0:512]
        act_sb = arena[:, 512:1024]
        scratch = arena[:, 1024 + 4 * H:]
        tile_in = [arena[:, 1024 + s * H:1024 + (s + 1) * H] for s in range(TRIO)]
        tile_out = [arena[:, 1024 + (s + 3) * H:1024 + (s + 4) * H] for s in range(TRIO)]

        GE = NG * E
        diff = stage[:, NG * P:(NG + 1) * P].bitcast(I32)
        after_b = sb("after_b", [P, P], BF16)
        same_e_b = sb("same_e_b", [P, P], BF16)
        earlier_b = sb("earlier_b", [P, P], BF16)
        ones_b = sb("ones_b", [P, 1], BF16)
        ints = scratch[:, 0:E + MAXT + E * E + NT].bitcast(I32)
        flts = sb("flts", [P, E + MAXT + E * E + NT])
        rev = flts[:, 0:E]
        full = flts[:, E:E + MAXT]
        before = flts[:, E + MAXT:E + MAXT + E * E].rearrange("p (e f) -> p e f", e=E)
        tile_no = flts[0:1, E + MAXT + E * E:]
        lg, lg2, tmp, rank = [scratch[:, i * GE:(i + 1) * GE].rearrange("p (g e) -> p g e", e=E) for i in range(4)]
        passed = scratch[0:1, 0:NT * E].rearrange("p (t e) -> p t e", e=E)
        oh = [sb(f"oh{k}", [P, NG, E]) for k in range(TOPK)]
        both_b = sb("both_b", [P, GE], BF16)
        totals_b = sb("totals_b", [P, P], BF16)
        top = sb("top", [P, TOPK, NG])
        best = sb("best", [P, NG])
        gap = sb("gap", [P, NG])
        expgap = sb("expgap", [P, NG])
        den = sb("den", [P, NG])
        score = sb("score", [P, TOPK, NG])
        posf = sb("posf", [P, TOPK, NG])
        pos = sb("pos", [P, TOPK, NG], I32)
        n_e = sb("n_e", [P, E])
        tiles_e = sb("tiles_e", [P, E])
        base_e = sb("base_e", [P, E])
        end_e = sb("end_e", [P, E])
        end_i = sb("end_i", [1, E], I32)
        tile_ef = scratch[0:1, 3 * GE:3 * GE + NT]
        tile_e = sb("tile_e", [1, NT // TRIO, TRIO + 1], I32)

        pG, pU, pX, pT = psum("pG"), psum("pU"), psum("pX"), psum("pT")
        pA = [psum(f"pA{i}") for i in range(GB)]

        itok_in = sem("itok_in")
        router_in = sem("router_in")
        x_in = [sem(f"x_in{b}") for b in range(NBLK)]
        cond_zeroed = sem("cond_zeroed")
        cond_gathered, cond_saved, cond_in = sem("cond_gathered"), sem("cond_saved"), sem("cond_in")
        gate_in, up_in, down_in = sem("gate_in"), sem("up_in"), sem("down_in")
        slots_zeroed = sem("slots_zeroed")
        zero_ready = sem("zero_ready")
        consts_ready = sem("consts_ready")
        pool_step = sem("pool_step")
        dve_step = sem("dve_step")
        y_mm = sem("y_mm")
        y_copied = [sem("y_copied_act"), sem("y_copied_dve")]
        yt_tr = sem("yt_tr")
        yt_hi, yt_lo = sem("yt_hi"), sem("yt_lo")
        router_zeroed = sem("router_zeroed")
        lgt_mm, lgt_copied = sem("lgt_mm"), sem("lgt_copied")
        router_hi, router_lo = sem("router_hi"), sem("router_lo")
        gate_hi, up_hi, down_hi = sem("gate_hi"), sem("up_hi"), sem("down_hi")
        gate_lo, up_lo, down_lo = sem("gate_lo"), sem("up_lo"), sem("down_lo")
        logits_mm = sem("logits_mm")
        gap_ready, expgap_ready = sem("gap_ready"), sem("expgap_ready")
        both_ready, prefix_mm, totals_ready, rank_mm = (
            sem("both_ready"), sem("prefix_mm"), sem("totals_ready"), sem("rank_mm"))
        route_ready = sem("route_ready")
        gate_mm, up_mm = sem("gate_mm"), sem("up_mm")
        silu_done, mul_done = sem("silu_done"), sem("mul_done")
        at_hi, at_lo = sem("at_hi"), sem("at_lo")
        acc_done = sem("acc_done")
        acc_added = sem("acc_added")
        stage_in, ew_h_in = sem("stage_in"), sem("ew_h_in")
        ew_split = sem("ew_split")
        scattered = sem("scattered")
        tile_loaded = [sem(f"tile_loaded{s}") for s in range(TRIO)]
        xt_tr, xt_hi, xt_lo = sem("xt_tr"), sem("xt_hi"), sem("xt_lo")
        at_tr = sem("at_tr")
        tile_mm = sem("tile_mm")
        tile_copied = sem("tile_copied")
        tile_stored = [sem(f"tile_stored{s}") for s in range(TRIO)]
        gathered = [sem(f"gathered{s}") for s in range(GWAY)]
        combined_first = sem("combined_first")
        combined = sem("combined")
        out_stored = sem("out_stored")

        block = ctx.enter_context(nc.Block())

        @block.sync
        def _(sp):
            def load_x(b):
                sp.dma_start(x_sb[:, b * GB:(b + 1) * GB, :],
                             x_rows[:, b * GB:(b + 1) * GB, :]).then_inc(x_in[b], 16)

            sp.dma_start(itok_sb[:, :], itok.rearrange("(b a) -> b a", a=1)).then_inc(itok_in, 16)
            load_x(0)
            sp.wait_ge(cond_gathered, 16)
            load_x(1)
            load_x(2)
            sp.wait_ge(cond_saved, 16)
            load_x(3)
            sp.dma_start(raw_a[:, :, :], w_gate.rearrange("(k p) n -> p k n", p=P)).then_inc(gate_in, 16)
            sp.dma_start(raw_b, w_up.rearrange("(k p) n -> p k n", p=P)).then_inc(up_in, 16)
            sp.wait_ge(gate_hi, 1)
            sp.wait_ge(gate_lo, 1)
            sp.dma_start(raw_a[:, :, :].rearrange("p k n -> p (k n)"),
                         w_down.rearrange("(c p) n -> p c n", p=P)).then_inc(down_in, 16)
            sp.wait_ge(zero_ready, 1)
            sp.dma_start(y_slots.rearrange("(t p) h -> p t h", p=P),
                         zero[:, :].unsqueeze(1).to_broadcast([P, NT + 1, H])).then_inc(slots_zeroed, 16)

            def load_tile(t, s):
                sp.dma_start(tile_in[s], y_slots[bass.ds(t * P, P), :]).then_inc(tile_loaded[s], 16)

            def store_tile(t, s):
                sp.wait_ge(tile_copied, t + 1)
                sp.dma_start(o_slots[bass.ds(t * P, P), :], tile_out[s]).then_inc(tile_stored[s], 16)

            sp.wait_ge(scattered, 16 * TOPK * NG)
            sp.wait_ge(up_hi, 1)
            sp.wait_ge(up_lo, 1)
            for s in range(TRIO):
                load_tile(s, s)
            with sp.Fori(0, NT // TRIO - 1) as i:
                for s in range(TRIO):
                    sp.wait_ge(xt_tr, i * TRIO + s + 1)
                    load_tile(i * TRIO + s + TRIO, s)
                    store_tile(i * TRIO + s, s)
            sp.wait_ge(xt_tr, NT - TRIO + 1)
            load_tile(NT, 0)
            for s in range(TRIO):
                store_tile(NT - TRIO + s, s)

            def store_groups(g, n):
                sp.dma_start(out_rows[:, bass.ds(g, n), :],
                             x_sb[:, bass.ds(g, n), :]).then_inc(out_stored, 16)

            for g in range(0, NG - GB, 2):
                sp.wait_ge(combined, g + 2)
                store_groups(g, 2)
            sp.wait_ge(combined, NG)
            for g in range(NG - GB, NG):
                sp.wait_ge(acc_added, g + 2)
                store_groups(g, 1)
            sp.wait_ge(out_stored, 16 * ((NG - GB) // 2 + GB))

        @block.gpsimd
        def _(pool):
            steps = [0]

            def then(ins):
                steps[0] += 1
                ins.then_inc(pool_step, 1)
                pool.wait_ge(pool_step, steps[0])

            nc.gpsimd.memset(stage[:, 0:NG * P], 0.0).then_inc(cond_zeroed, 1)
            pool.wait_ge(itok_in, 16)
            pool.indirect_dma_start(
                out=cond_sb, out_offset=None, in_=cond_w.rearrange("s c d -> s (c d)"),
                in_offset=bass.IndirectOffsetOnAxis(ap=itok_sb[:, 0:1], axis=0)).then_inc(cond_gathered, 16)
            then(nc.gpsimd.memset(ident[:, :], 0.0))
            nc.gpsimd.affine_select(out=ident[:, :], in_=ident[:, :], compare_op=ALU.not_equal, fill=1.0,
                                    base=0, pattern=[[-1, P]], channel_multiplier=1).then_inc(consts_ready, 1)
            pool.wait_ge(cond_gathered, 16)
            pool.dma_start(cond_rows, cond_sb).then_inc(cond_saved, 16)
            nc.gpsimd.memset(ones_b[:, :], 1.0).then_inc(consts_ready, 1)
            nc.gpsimd.iota(diff, pattern=[[1, P]], base=P, channel_multiplier=-1).then_inc(consts_ready, 1)
            col = 0
            for pattern, base in (([[-1, E]], E), ([[P, MAXT]], 0), ([[1, E], [-1, E]], 0), ([[1, NT]], 0)):
                n = pattern[0][1] * (pattern[1][1] if len(pattern) > 1 else 1)
                nc.gpsimd.iota(ints[:, col:col + n], pattern=pattern, base=base,
                               channel_multiplier=0).then_inc(consts_ready, 1)
                col += n
            pool.wait_ge(cond_saved, 16)
            pool.wait_ge(cond_zeroed, 1)
            for j in range(BPG):
                pool.dma_start(cond_blk[C * j:C * j + C, :, C * j:C * j + C],
                               cond_rows.rearrange("(g j) (c d) -> j c g d", j=BPG, d=C)[j]).then_inc(cond_in, 16)
            nc.gpsimd.memset(zero[:, :], 0.0).then_inc(zero_ready, 1)

            def load_expert(dst, e, done):
                pool.dma_start(dst[:, 0:WCOL].rearrange("p (k n) -> p k n", k=KC),
                               w1[e].rearrange("(k p) n -> p k n", p=P)).then_inc(done, 16)
                pool.dma_start(dst[:, WCOL:ECOL].rearrange("p (i n) -> p i n", i=IC),
                               w2[e].rearrange("(i p) n -> p i n", p=P)).then_inc(done, 16)

            def split_expert(e):
                if e >= 2:
                    last = pool.value_load(end_i[0:1, e - 2:e - 1], min_val=1, max_val=NT)
                pool.wait_ge(stage_in, 32 * (e + 1))
                if e >= 2:
                    pool.wait_ge(tile_mm, last)
                load_expert(ew_h[:, e % 2, :], e, ew_h_in)
                pool.wait_ge(ew_h_in, 32 * (e + 1))
                nc.gpsimd.tensor_tensor(ew_l[:, e % 2, :], stage[:, :], ew_h[:, e % 2, :],
                                        ALU.subtract).then_inc(ew_split, 1)
                if e < E - 1:
                    pool.wait_ge(ew_split, e + 1)
                    load_expert(stage[:, :], e + 1, stage_in)

            pool.wait_ge(logits_mm, 1)
            load_expert(stage[:, :], 0, stage_in)
            split_expert(0)

            pool.wait_ge(route_ready, 1)
            pool.wait_ge(slots_zeroed, 16)
            for g in range(NG):
                for k in range(TOPK):
                    pool.indirect_dma_start(
                        out=y_slots, out_offset=bass.IndirectOffsetOnAxis(ap=pos[:, k, g:g + 1], axis=0),
                        in_=y_sb[:, g, :], in_offset=None).then_inc(scattered, 16)
            for e in range(1, E):
                split_expert(e)

            for s in range(TRIO):
                pool.wait_ge(tile_stored[s], 16 * (NT // TRIO))
            for g in range(NG):
                if g >= GWAY:
                    pool.wait_ge(combined, g - GWAY + 1)
                for k in range(TOPK):
                    pool.indirect_dma_start(
                        out=y_sb[:, TOPK * (g % GWAY) + k, :], out_offset=None, in_=o_slots,
                        in_offset=bass.IndirectOffsetOnAxis(ap=pos[:, k, g:g + 1], axis=0)
                    ).then_inc(gathered[g % GWAY], 16)

        @block.scalar
        def _(act):
            act.dma_start(rt_raw[:, :, :], router_w.rearrange("(k p) e -> p k e", p=P)).then_inc(router_in, 16)
            act.wait_ge(router_in, 16)
            act.wait_ge(router_zeroed, 2)
            nc.scalar.copy(rt_h[:, :, 0:E], rt_raw[:, :, :]).then_inc(router_hi, 1)
            act.wait_ge(gate_in, 16)
            nc.scalar.copy(gu_h[:, :, 0:SH], raw_a[:, :, :]).then_inc(gate_hi, 1)
            act.wait_ge(up_in, 16)
            nc.scalar.copy(gu_h[:, :, SH:2 * SH], raw_b).then_inc(up_hi, 1)

            def split_yt(b):
                pair = (pX, pT) if b % 2 == 0 else (pG, pU)
                act.wait_ge(yt_tr, b + 1)
                for k in range(KC):
                    nc.scalar.copy(yt_h[:, k, b * BLK:(b + 1) * BLK], pair[k][:, :]).then_inc(yt_hi, 1)

            for b in range(NBLK):
                act.wait_ge(y_mm, 2 * b + 1)
                nc.scalar.copy(y_sb[:, b * GB:b * GB + 2, :],
                               pA[2 * (b % 2)][:, :]).then_inc(y_copied[0], 1)
                if b >= 1:
                    split_yt(b - 1)
            split_yt(NBLK - 1)
            act.wait_ge(up_lo, 1)
            for b in range(NBLK):
                act.wait_ge(lgt_mm, b + 1)
                nc.scalar.copy(lgt[b], pA[b][0:E, :]).then_inc(lgt_copied, 1)
            act.wait_ge(down_in, 16)
            nc.scalar.copy(wd_h[:, :, :], raw_a[:, :, :].rearrange("p k n -> p (k n)")
                           .rearrange("p (c n) -> p c n", c=SC)).then_inc(down_hi, 1)

            def silu(u):
                act.wait_ge(gate_mm, u + 1)
                nc.scalar.activation(silu_sb, pG[:, :], ACT.Silu).then_inc(silu_done, 1)

            def shared_block(u, routing=False):
                for c in range(SC):
                    silu(u + c)
                    act.wait_ge(mul_done, u + (c + 2))
                    nc.scalar.copy(at_h[:, c % 2, :], act_sb).then_inc(at_hi, 1)
                    if routing and c == 1:
                        act.wait_ge(gap_ready, 1)
                        nc.scalar.activation(expgap[:, :], gap[:, :], ACT.Exp, scale=-1.0).then_inc(expgap_ready, 1)

            def split_xt(t):
                act.wait_ge(xt_tr, t + 1)
                nc.scalar.copy(xt_h[:, :, :], pX[:, 0:KC * P]).then_inc(xt_hi, 1)

            def copy_out(t, s):
                act.wait_ge(tile_mm, t + 1)
                nc.scalar.copy(tile_out[s], pA[0][:, 0:H]).then_inc(tile_copied, 1)

            def expert_tile(t, s, first=False, stored=None):
                silu(t + S1)
                split_xt(t + 1)
                act.wait_ge(at_tr, t + 1)
                nc.scalar.copy(at_h[:, 0, :], pT[:, :]).then_inc(at_hi, 1)
                if not first:
                    if stored is not None:
                        act.wait_ge(tile_stored[(s - 1) % TRIO], stored)
                    copy_out(t - 1, (s - 1) % TRIO)

            shared_block(0, routing=True)
            for b in range(1, HALF):
                shared_block(b * SC)
            split_xt(0)
            for t in range(TRIO + 1):
                expert_tile(t, t % TRIO, first=(t == 0))
            for t in range(TRIO + 1, 2 * TRIO):
                expert_tile(t, t % TRIO, stored=16)
            with act.Fori(2, NT // TRIO) as i:
                for s in range(TRIO):
                    expert_tile(i * TRIO + s, s, stored=i * 16 if s else i * 16 - 16)
            act.wait_ge(tile_stored[TRIO - 1], 16 * (NT // TRIO - 1))
            copy_out(NT - 1, TRIO - 1)
            with act.Fori(0, HALF) as n:
                shared_block(n * SC + S2)

        @block.vector
        def _(dve):
            steps = [0]

            def then(ins):
                steps[0] += 1
                ins.then_inc(dve_step, 1)
                dve.wait_ge(dve_step, steps[0])

            V = nc.vector
            V.memset(rt_h[:, :, :].bitcast(F32), 0.0).then_inc(router_zeroed, 1)
            V.memset(rt_l[:, :, :].bitcast(F32), 0.0).then_inc(router_zeroed, 1)
            dve.wait_ge(consts_ready, 7)
            then(V.tensor_single_scalar(after_b[:, :], diff, P, ALU.is_gt))
            then(V.tensor_single_scalar(diff, diff, E - 1, ALU.bitwise_and))
            then(V.tensor_single_scalar(same_e_b[:, :], diff, 0, ALU.is_equal))
            V.tensor_tensor(earlier_b[:, :], after_b[:, :], same_e_b[:, :], ALU.mult)
            then(V.tensor_copy(flts[:, :], ints))
            V.memset(full[:, 0:1], -1.0).then_inc(mul_done, 1)
            V.memset(posf[:, 0, :], 0.0).then_inc(at_lo, 1)
            V.memset(posf[:, 1, :], 0.0).then_inc(acc_added, 1)
            then(V.tensor_scalar(before, before, 0.0, float(P), ALU.is_gt, ALU.mult))

            dve.wait_ge(router_hi, 1)
            dve.wait_ge(router_zeroed, 2)
            V.tensor_tensor(rt_l[:, :, 0:E], rt_raw[:, :, :], rt_h[:, :, 0:E], ALU.subtract).then_inc(router_lo, 1)
            dve.wait_ge(gate_hi, 1)
            V.tensor_tensor(gu_l[:, :, 0:SH], raw_a[:, :, :], gu_h[:, :, 0:SH], ALU.subtract).then_inc(gate_lo, 1)
            dve.wait_ge(up_hi, 1)
            V.tensor_tensor(gu_l[:, :, SH:2 * SH], raw_b, gu_h[:, :, SH:2 * SH], ALU.subtract).then_inc(up_lo, 1)

            def split_yt(b):
                pair = (pX, pT) if b % 2 == 0 else (pG, pU)
                for k in range(KC):
                    dve.wait_ge(yt_hi, b * KC + k + 1)
                    cols = slice(b * BLK, (b + 1) * BLK)
                    V.tensor_tensor(yt_l[:, k, cols], pair[k][:, :], yt_h[:, k, cols],
                                    ALU.subtract).then_inc(yt_lo, 1)

            for b in range(NBLK):
                dve.wait_ge(y_mm, 2 * b + 2)
                V.tensor_copy(y_sb[:, b * GB + 2:(b + 1) * GB, :],
                              pA[2 * (b % 2) + 1][:, :]).then_inc(y_copied[1], 1)
                if b >= 1:
                    split_yt(b - 1)
            split_yt(NBLK - 1)
            def bc(a):
                return a.unsqueeze(2).to_broadcast([P, NG, E])

            rev_all = rev.unsqueeze(1).to_broadcast([P, NG, E])

            def pick(k, values):
                then(V.reduce_max(top[:, k, :], values[:, :, :], AX.X))
                then(V.tensor_tensor(tmp, values[:, :, :], bc(top[:, k, :]), ALU.is_equal))
                then(V.tensor_tensor(tmp, tmp, rev_all, ALU.mult))
                then(V.reduce_max(best[:, :], tmp, AX.X))
                then(V.tensor_tensor(oh[k][:, :, :], rev_all, bc(best[:, :]), ALU.is_equal))

            dve.wait_ge(down_hi, 1)
            V.tensor_tensor(wd_l[:, :, :], raw_a[:, :, :].rearrange("p k n -> p (k n)")
                            .rearrange("p (c n) -> p c n", c=SC), wd_h[:, :, :], ALU.subtract).then_inc(down_lo, 1)

            def choose():
                dve.wait_ge(logits_mm, 1)
                then(V.tensor_copy(lg, pX[:, 0:GE]))
                pick(0, lg)
                then(V.scalar_tensor_tensor(out=lg2, in0=oh[0][:, :, :], scalar=-3.0e38, in1=lg,
                                            op0=ALU.mult, op1=ALU.add))
                pick(1, lg2)
                V.tensor_tensor(both_b[:, :], oh[0][:, :, :].rearrange("p g e -> p (g e)"),
                                oh[1][:, :, :].rearrange("p g e -> p (g e)"), ALU.add).then_inc(both_ready, 1)
                V.tensor_tensor(gap[:, :], top[:, 0, :], top[:, 1, :], ALU.subtract).then_inc(gap_ready, 1)

            def totals():
                dve.wait_ge(prefix_mm, 1)
                V.tensor_copy(totals_b[:, :], pT[:, 0:1].to_broadcast([P, P])).then_inc(totals_ready, 1)

            def place():
                dve.wait_ge(rank_mm, 1)
                then(V.tensor_copy(n_e[:, :], pT[:, 0:E]))
                more = tmp.rearrange("p g e -> p (g e)").rearrange("p (e j) -> p e j", e=E)
                then(V.tensor_tensor(more, n_e[:, :].unsqueeze(2).to_broadcast([P, E, MAXT]),
                                     full.unsqueeze(1).to_broadcast([P, E, MAXT]), ALU.is_gt))
                then(V.tensor_reduce(out=tiles_e[:, :], in_=more, axis=AX.X, op=ALU.add))
                sums = lg2[:, 0:E, :]
                then(V.tensor_tensor(sums, before, tiles_e[:, :].unsqueeze(1).to_broadcast([P, E, E]), ALU.mult))
                then(V.tensor_reduce(out=base_e[:, :], in_=sums, axis=AX.X, op=ALU.add))
                then(V.tensor_tensor(rank, pX[:, 0:GE].rearrange("p (g e) -> p g e", e=E),
                                     base_e[:, :].unsqueeze(1).to_broadcast([P, NG, E]), ALU.add))
                for k in range(TOPK):
                    then(V.tensor_tensor(tmp, oh[k][:, :, :], rank, ALU.mult))
                    then(V.tensor_reduce(out=posf[:, k, :], in_=tmp, axis=AX.X, op=ALU.add))
                then(V.tensor_copy(pos[:, :, :], posf[:, :, :]))
                then(V.scalar_tensor_tensor(out=end_e[:, :], in0=base_e[:, :], scalar=1.0 / P, in1=tiles_e[:, :],
                                            op0=ALU.mult, op1=ALU.add))
                then(V.tensor_tensor(passed, end_e[0:1, :].unsqueeze(1).to_broadcast([1, NT, E]),
                                     tile_no.unsqueeze(2).to_broadcast([1, NT, E]), ALU.is_le))
                then(V.tensor_reduce(out=tile_ef, in_=passed, axis=AX.X, op=ALU.add))
                then(V.tensor_scalar_min(tile_ef, tile_ef, float(E - 1)))
                trios = tile_ef.rearrange("p (i s) -> p i s", s=TRIO)
                V.tensor_copy(tile_e[:, :, 1:], trios)
                V.memset(tile_e[:, 0, 0:1], 0)
                then(V.tensor_copy(tile_e[:, 1:, 0:1], trios[:, 0:NT // TRIO - 1, TRIO - 1:TRIO]))
                V.tensor_copy(end_i[:, :], end_e[0:1, :]).then_inc(route_ready, 1)

            def softmax():
                dve.wait_ge(expgap_ready, 1)
                then(V.tensor_scalar_add(den[:, :], expgap[:, :], 1.0))
                then(V.reciprocal(score[:, 0, :], den[:, :]))
                then(V.tensor_tensor(score[:, 1, :], score[:, 0, :], expgap[:, :], ALU.mult))

            def gated(u):
                dve.wait_ge(up_mm, u + 1)
                dve.wait_ge(silu_done, u + 1)
                V.tensor_tensor(act_sb, pU[:, :], silu_sb, ALU.mult).then_inc(mul_done, 1)

            def shared_block(u, g0, pieces={}, n=None):
                for c in range(SC):
                    dve.wait_ge(at_lo, u + (c + 1))
                    gated(u + c)
                    dve.wait_ge(at_hi, u + (c + 1))
                    V.tensor_tensor(at_l[:, c % 2, :], act_sb, at_h[:, c % 2, :],
                                    ALU.subtract).then_inc(at_lo, 1)
                    if c in pieces:
                        pieces[c]()
                    if n is not None and c >= SC // 2:
                        for g in (2 * (c - SC // 2), 2 * (c - SC // 2) + 1):
                                dve.wait_ge(gathered[g], n * 32 + 32)
                                xg = x_sb[:, bass.ds(n * GWAY + g, 1), :].rearrange("p a h -> p (a h)")
                                for k, done in enumerate((combined_first, combined)):
                                    w = score[:, k, bass.ds(n * GWAY + g, 1)]
                                    V.scalar_tensor_tensor(out=xg, in0=y_sb[:, TOPK * g + k, :], scalar=w,
                                                           in1=xg, op0=ALU.mult, op1=ALU.add).then_inc(done, 1)
                                    if k == 0:
                                        dve.wait_ge(combined_first, n * GWAY + (g + 1))
                if n is not None:
                    dve.wait_ge(combined, n * GWAY + GWAY)
                for q in range(GB):
                    dve.wait_ge(acc_done, g0 + (q + 1))
                    xg = x_sb[:, bass.ds(g0 + q, 1), :].rearrange("p a h -> p (a h)")
                    V.tensor_tensor(xg, pA[q][:, 0:H], xg, ALU.add).then_inc(acc_added, 1)

            def split_xt(t):
                dve.wait_ge(xt_hi, t + 1)
                V.tensor_tensor(xt_l[:, :, :], pX[:, 0:KC * P], xt_h[:, :, :].rearrange("p k t -> p (k t)"),
                                ALU.subtract).then_inc(xt_lo, 1)

            shared_block(0, 0, pieces={0: choose, 1: totals, 2: place, 3: softmax})
            for b in range(1, HALF):
                shared_block(b * SC, b * GB)
            split_xt(0)
            with dve.Fori(0, NT) as t:
                gated(t + S1)
                split_xt(t + 1)
                dve.wait_ge(at_hi, t + (S1 + 1))
                V.tensor_tensor(at_l[:, 0, :], pT[:, :], at_h[:, 0, :], ALU.subtract).then_inc(at_lo, 1)
            with dve.Fori(0, HALF) as n:
                shared_block(n * SC + S2, n * GB + HALF * GB, n=n)

        @block.tensor
        def _(pe):
            mm = nc.tensor.matmul

            def product(dst, pairs):
                n = 0
                for wh, wl, vh, vl in pairs:
                    for a, b in ((wh, vh), (wh, vl), (wl, vh)):
                        last = mm(dst, a, b, start=(n == 0), stop=(n == 3 * len(pairs) - 1))
                        n += 1
                return last

            def y_block(b):
                pe.wait_ge(x_in[b], 16)
                if b >= 2:
                    pe.wait_ge(y_copied[0], b - 1)
                    pe.wait_ge(y_copied[1], b - 1)
                for q in range(GB):
                    g = b * GB + q
                    last = mm(pA[2 * (b % 2) + q // 2][:, (q % 2) * H:(q % 2 + 1) * H], cond_blk[:, g, :],
                              x_sb[:, g, :], start=True, stop=True)
                    if q % 2 == 1:
                        last.then_inc(y_mm, 1)

            def transpose_block(b):
                pair = (pX, pT) if b % 2 == 0 else (pG, pU)
                pe.wait_ge(y_copied[0], b + 1)
                pe.wait_ge(y_copied[1], b + 1)
                if b >= 2:
                    pe.wait_ge(yt_lo, KC * (b - 1))
                for q in range(GB):
                    for k in range(KC):
                        last = nc.tensor.transpose(pair[k][:, q * P:(q + 1) * P],
                                                   y_sb[:, b * GB + q, k * P:(k + 1) * P], ident[:, :])
                last.then_inc(yt_tr, 1)

            pe.wait_ge(consts_ready, 1)
            pe.wait_ge(cond_in, 16 * BPG)
            for b in range(NBLK):
                y_block(b)
                if b >= 1:
                    transpose_block(b - 1)
            transpose_block(NBLK - 1)

            pe.wait_ge(router_lo, 1)
            for b in range(NBLK):
                pe.wait_ge(yt_lo, KC * (b + 1))
                cols = slice(b * BLK, (b + 1) * BLK)
                product(pA[b][:, :], [(rt_h[:, k, :], rt_l[:, k, :], yt_h[:, k, cols], yt_l[:, k, cols])
                                      for k in range(KC)]).then_inc(lgt_mm, 1)

            def logits():
                pe.wait_ge(lgt_copied, NBLK)
                for g in range(NG):
                    q = g % GB
                    last = nc.tensor.transpose(pX[:, g * E:(g + 1) * E], lgt[g // GB][:, q * P:(q + 1) * P],
                                               ident[0:E, 0:E])
                last.then_inc(logits_mm, 1)

            def prefix():
                pe.wait_ge(both_ready, 1)
                mm(pT[:, 0:1], both_b[:, :], ones_b[:, :], start=True, stop=True).then_inc(prefix_mm, 1)

            def ranks():
                pe.wait_ge(totals_ready, 1)
                mm(pX[:, 0:GE], after_b[:, :], both_b[:, :], start=True, stop=False)
                mm(pX[:, 0:GE], totals_b[:, :], earlier_b[:, :], start=False, stop=True)
                mm(pT[:, 0:E], totals_b[:, :], same_e_b[:, 0:E], start=True, stop=True).then_inc(rank_mm, 1)

            def shared_block(u, tok0, added, pieces={}):
                def down(c):
                    pe.wait_ge(at_lo, u + (c + 2))
                    if c == 0:
                        pe.wait_ge(acc_added, added)
                    for q in range(GB):
                        tok = slice(q * P, (q + 1) * P)
                        for i, (a, b) in enumerate(((at_h, wd_h), (at_h, wd_l), (at_l, wd_h))):
                            last = mm(pA[q][:, 0:H], a[:, c % 2, tok], b[:, c, :],
                                      start=(c == 0 and i == 0), stop=(c == SC - 1 and i == 2))
                        if c == SC - 1:
                            last.then_inc(acc_done, 1)

                def moving(y, k):
                    return y[:, k, bass.ds(tok0, BLK)]

                for c in range(SC):
                    pe.wait_ge(mul_done, u + (c + 1))
                    for dst, at, done in ((pG, 0, gate_mm), (pU, SH, up_mm)):
                        cols = slice(at + c * P, at + (c + 1) * P)
                        product(dst[:, :], [(gu_h[:, k, cols], gu_l[:, k, cols], moving(yt_h, k),
                                             moving(yt_l, k)) for k in range(KC)]).then_inc(done, 1)
                    if c in pieces:
                        pieces[c]()
                    if c == 1:
                        for done in (down_lo, ) if pieces else ():
                            pe.wait_ge(done, 1)
                    if c >= 1:
                        down(c - 1)
                down(SC - 1)

            def transpose_tile(t, s, i):
                pe.wait_ge(tile_loaded[s], i * 16 + 16)
                pe.wait_ge(xt_lo, t)
                for k in range(KC):
                    last = nc.tensor.transpose(pX[:, k * P:(k + 1) * P], tile_in[s][:, k * P:(k + 1) * P],
                                               ident[:, :])
                last.then_inc(xt_tr, 1)

            def expert_weights(w, place, lo, n):
                return w[:, bass.ds(place, 1), lo:lo + n].rearrange("p a n -> p (a n)")

            def tile_second(t, place):
                pe.wait_ge(at_lo, t + (S1 + 2))
                pe.wait_ge(tile_copied, t)
                product(pA[0][:, 0:H],
                        [(at_h[:, 0, i * P:(i + 1) * P], at_l[:, 0, i * P:(i + 1) * P],
                          expert_weights(ew_h, place, WCOL + i * H, H), expert_weights(ew_l, place, WCOL + i * H, H))
                         for i in range(IC)]).then_inc(tile_mm, 1)

            def experts_of(i):
                _, experts = nc.values_load_multi_w_load_instructions(
                    tile_e[0:1, bass.ds(i, 1), :].rearrange("p a s -> p (a s)"), engines=[pe.engine],
                    min_val=0, max_val=E - 1)
                return experts, [pe.snap(e & 1) for e in experts]

            def expert_tile(t, s, i, experts, places, first=False):
                expert, place = experts[s + 1], places[s + 1]
                pe.wait_ge(ew_split, expert + 1)
                pe.wait_ge(xt_lo, t + 1)
                for dst, at, done in ((pG, 0, gate_mm), (pU, INTER, up_mm)):
                    product(dst[:, :],
                            [(xt_h[:, k, :], xt_l[:, k, :],
                              expert_weights(ew_h, place, k * 2 * INTER + at, INTER),
                              expert_weights(ew_l, place, k * 2 * INTER + at, INTER))
                             for k in range(KC)]).then_inc(done, 1)
                transpose_tile(t + 1, (s + 1) % TRIO, i if s < TRIO - 1 else i + 1)
                if not first:
                    tile_second(t - 1, places[s])
                pe.wait_ge(mul_done, t + (S1 + 2))
                for c in range(IC):
                    last = nc.tensor.transpose(pT[:, c * P:(c + 1) * P], act_sb[:, c * P:(c + 1) * P], ident[:, :])
                last.then_inc(at_tr, 1)

            pe.wait_ge(gate_lo, 1)
            pe.wait_ge(up_lo, 1)
            shared_block(0, 0, 1, pieces={0: logits, 1: prefix, 2: ranks})
            for b in range(1, HALF):
                shared_block(b * SC, b * BLK, b * GB + 1)
            pe.wait_ge(route_ready, 1)
            transpose_tile(0, 0, 0)
            pe.wait_ge(acc_added, HALF * GB + 1)
            experts, places = experts_of(0)
            for s in range(TRIO):
                expert_tile(s, s, 0, experts, places, first=(s == 0))
            with pe.Fori(1, NT // TRIO) as i:
                experts, places = experts_of(i)
                for s in range(TRIO):
                    expert_tile(i * TRIO + s, s, i, experts, places)
            _, places = experts_of(NT // TRIO - 1)
            tile_second(NT - 1, places[TRIO])
            pe.wait_ge(tile_copied, NT)
            with pe.Fori(0, HALF) as n:
                shared_block(n * SC + S2, n * BLK + HALF * BLK, n * GB + (HALF * GB + 1))


_INS = ['x', 'itok_B_1_198', 'L0_cond_weights', 'L0_ffn_router_w', 'L0_ffn_w1', 'L0_ffn_w2',
        'L0_ffn_w_gate', 'L0_ffn_w_up', 'L0_ffn_w_down']


def kernel(**inputs):
    import numpy as _np
    import concourse.bacc as _bacc
    from concourse import mybir as _mybir
    from concourse.bass_utils import run_bass_kernel_spmd as _run

    nc = _bacc.Bacc("TRN2", target_bir_lowering=False, num_devices=1)
    arrays, args = {}, []
    for name in _INS:
        a = _np.ascontiguousarray(inputs[name])
        arrays[f"in_{name}_dram"] = a
        args.append(nc.dram_tensor(f"in_{name}_dram", a.shape, _mybir.dt.from_np(a.dtype), kind="ExternalInput").ap())
    shape = inputs['x'].shape
    out = nc.dram_tensor("out_0_dram", shape, _mybir.dt.float32, kind="ExternalOutput").ap()
    cond_moe_ffn(nc, *args, out)
    r = _run(nc, [arrays], core_ids=[0])
    return r.results[0]["out_0_dram"]
```
